# Optimizing a Trainium2 kernel written in Bass

```python
import numpy as np
import jax
import jax.numpy as jnp

def _softmax(x, axis=-1):
    return jax.nn.softmax(x, axis=axis)

def _gelu(x):
    return jax.nn.gelu(x, approximate=True)

def _silu(x):
    return jax.nn.silu(x)

def _sigmoid(x):
    return jax.nn.sigmoid(x)

def _layernorm(x, axis=-1, eps=1e-05):
    m = jnp.mean(x, axis=axis, keepdims=True)
    v = jnp.var(x, axis=axis, keepdims=True)
    return (x - m) / jnp.sqrt(v + eps)

def _scatter_add(tgt, idx, src, axis=0):
    return tgt.at[idx].add(src)

def _segment_sum(src, seg, n):
    return jax.ops.segment_sum(src, seg, n)
kernel_name = 'mk_gnn_preln_d2_gnn_r8_118a41'

def setup_inputs(seed: int=0):
    np.random.seed(seed)
    _w = jnp.asarray

    def _rec_inputs():
        import jax
        import jax.numpy as jnp
        _gk = jax.random.key(seed)
        x = -0.0003713 + 1 * jax.random.normal(jax.random.fold_in(_gk, 1), (12500, 128), jnp.float32)
        src = jax.random.randint(jax.random.fold_in(_gk, 2), (200000,), 0, 12500, jnp.int32)
        dst = jax.random.randint(jax.random.fold_in(_gk, 3), (200000,), 0, 12500, jnp.int32)
        _o = jnp.argsort(dst, stable=True)
        src = src[_o]
        dst = dst[_o]
        edge_attr_50 = 0.000164634 + 1.0002 * jax.random.normal(jax.random.fold_in(_gk, 11), (200000, 50), jnp.float32)
        return (x, src, dst, edge_attr_50)
    x, src, dst, edge_attr_50 = _rec_inputs()

    def _L0_gnn_setup():
        import jax, jax.numpy as jnp
        import numpy as np
        N_NODES = 12500
        key = jax.random.key(seed)
        k1, k2, k3, k4, k5 = jax.random.split(key, 5)
        in_dim, out_dim = (128, 128)
        x = jax.random.normal(k1, (N_NODES, in_dim), dtype=jnp.float32)
        edge_index = jax.random.randint(k2, (2, 75000), 0, N_NODES, dtype=jnp.int64)
        s = 1.0 / np.sqrt(in_dim)
        W_rel = jax.random.uniform(k3, (out_dim, in_dim), jnp.float32, -s, s)
        W_root = jax.random.uniform(k4, (out_dim, in_dim), jnp.float32, -s, s)
        b_rel = jax.random.uniform(k5, (out_dim,), jnp.float32, -s, s)
        return {'x': x, 'edge_index': edge_index, 'W_rel': W_rel, 'W_root': W_root, 'b_rel': b_rel}
    _L0_gnn_all = _L0_gnn_setup()
    _L0_gnn_in = {k: v for k, v in _L0_gnn_all.items() if k in ('W_rel', 'W_root', 'b_rel')}
    del _L0_gnn_all

    def _L1_gnn_setup():
        import jax, jax.numpy as jnp
        import numpy as np
        N_NODES = 6250
        N_EDGES = 100000
        NODE_DIM = 128
        EDGE_DIM = 50
        HIDDEN_DIM = 128

        def _linear_params(key, fan_in, fan_out):
            kw, kb = jax.random.split(key)
            bound = 1.0 / np.sqrt(fan_in)
            W = jax.random.uniform(kw, (fan_in, fan_out), minval=-bound, maxval=bound, dtype=jnp.float32)
            b = jax.random.uniform(kb, (fan_out,), minval=-bound, maxval=bound, dtype=jnp.float32)
            return (W, b)
        key = jax.random.key(seed)
        ks = jax.random.split(key, 7)
        x = jax.random.normal(ks[0], (N_NODES, NODE_DIM), dtype=jnp.float32)
        edge_index = jax.random.randint(ks[1], (2, N_EDGES), 0, N_NODES, dtype=jnp.int64)
        edge_features = jax.random.normal(ks[2], (N_EDGES, EDGE_DIM), dtype=jnp.float32)
        We1, be1 = _linear_params(ks[3], EDGE_DIM, HIDDEN_DIM)
        We2, be2 = _linear_params(ks[4], HIDDEN_DIM, NODE_DIM)
        Wn1, bn1 = _linear_params(ks[5], NODE_DIM, HIDDEN_DIM)
        Wn2, bn2 = _linear_params(ks[6], HIDDEN_DIM, NODE_DIM)
        return {'x': x, 'edge_index': edge_index, 'edge_features': edge_features, 'We1': We1, 'be1': be1, 'We2': We2, 'be2': be2, 'Wn1': Wn1, 'bn1': bn1, 'Wn2': Wn2, 'bn2': bn2}
    _L1_gnn_all = _L1_gnn_setup()
    _L1_gnn_in = {k: v for k, v in _L1_gnn_all.items() if k in ('We1', 'be1', 'We2', 'be2', 'Wn1', 'bn1', 'Wn2', 'bn2')}
    del _L1_gnn_all
    return {'x': x, 'src': src, 'dst': dst, 'edge_attr_50': edge_attr_50, 'L0_gnn_W_rel': _L0_gnn_in['W_rel'], 'L0_gnn_W_root': _L0_gnn_in['W_root'], 'L0_gnn_b_rel': _L0_gnn_in['b_rel'], 'L1_gnn_We1': _L1_gnn_in['We1'], 'L1_gnn_be1': _L1_gnn_in['be1'], 'L1_gnn_We2': _L1_gnn_in['We2'], 'L1_gnn_be2': _L1_gnn_in['be2'], 'L1_gnn_Wn1': _L1_gnn_in['Wn1'], 'L1_gnn_bn1': _L1_gnn_in['bn1'], 'L1_gnn_Wn2': _L1_gnn_in['Wn2'], 'L1_gnn_bn2': _L1_gnn_in['bn2']}

def reference(x, src, dst, edge_attr_50, L0_gnn_W_rel, L0_gnn_W_root, L0_gnn_b_rel, L1_gnn_We1, L1_gnn_be1, L1_gnn_We2, L1_gnn_be2, L1_gnn_Wn1, L1_gnn_bn1, L1_gnn_Wn2, L1_gnn_bn2):
    import jax
    import jax.numpy as jnp

    def _L0_gnn_ref(x, edge_index, W_rel, W_root, b_rel):
        import jax, jax.numpy as jnp
        import numpy as np
        N_NODES = 12500
        src, dst = (edge_index[0], edge_index[1])
        agg = jax.ops.segment_sum(x[src], dst, num_segments=N_NODES)
        out = agg @ W_rel.T + b_rel + x @ W_root.T
        return out

    def _L1_gnn_ref(x, edge_index, edge_features, We1, be1, We2, be2, Wn1, bn1, Wn2, bn2):
        import jax, jax.numpy as jnp
        import numpy as np
        N_NODES = 6250
        N_EDGES = 100000
        NODE_DIM = 128
        EDGE_DIM = 50
        HIDDEN_DIM = 128

        def _linear_params(key, fan_in, fan_out):
            kw, kb = jax.random.split(key)
            bound = 1.0 / np.sqrt(fan_in)
            W = jax.random.uniform(kw, (fan_in, fan_out), minval=-bound, maxval=bound, dtype=jnp.float32)
            b = jax.random.uniform(kb, (fan_out,), minval=-bound, maxval=bound, dtype=jnp.float32)
            return (W, b)
        src = edge_index[0]
        dst = edge_index[1]
        edge_weights = jax.nn.silu(edge_features @ We1 + be1) @ We2 + be2
        messages = x[src] * edge_weights
        agg = jax.ops.segment_sum(messages, dst, num_segments=x.shape[0])
        out = jax.nn.silu(agg @ Wn1 + bn1) @ Wn2 + bn2
        return x + out
    edge_index = jnp.stack([src, dst])
    h = jnp.maximum(_layernorm(x, axis=-1), 0.0)
    x = x + _L0_gnn_ref(h, edge_index, L0_gnn_W_rel, L0_gnn_W_root, L0_gnn_b_rel)
    h = jnp.maximum(_layernorm(x, axis=-1), 0.0)
    x = x + _L1_gnn_ref(h, edge_index, edge_attr_50, L1_gnn_We1, L1_gnn_be1, L1_gnn_We2, L1_gnn_be2, L1_gnn_Wn1, L1_gnn_bn1, L1_gnn_Wn2, L1_gnn_bn2)
    return x

_drawn_inputs = setup_inputs


def setup_inputs(seed=0):
    import zlib

    import numpy as np

    out = dict(_drawn_inputs(seed))
    spreads = {}
    factors = {'edge_attr_50': 2.882,
     'L0_gnn_b_rel': 4.329,
     'L1_gnn_We1': 2.889,
     'L1_gnn_be1': 5.085,
     'L1_gnn_bn1': 8.0,
     'L1_gnn_bn2': 5.544}
    for name, (base, spread) in spreads.items():
        noise = np.random.default_rng([zlib.crc32(name.encode()), seed]).standard_normal(out[name].shape)
        drawn = base * np.exp(spread * noise) if base else spread * noise
        out[name] = jnp.asarray(drawn.astype(out[name].dtype))
    for name, factor in factors.items():
        out[name] = (out[name] * factor).astype(out[name].dtype)
    return out
```

```python
from contextlib import ExitStack

import concourse.bass as bass
from concourse import mybir

F32 = mybir.dt.float32
I32 = mybir.dt.int32
ALU = mybir.AluOpType
ACT = mybir.ActivationFunctionType
AX = mybir.AxisListType

P = 128
N_NODES = 12500
N_EDGES = 200000
D = 128
D_EDGE = 50
EPS = 1e-5
TB = 4
BLOCK = TB * P
N_BLOCKS = -(-N_EDGES // BLOCK)
U = 17
ITERS = N_BLOCKS // U
assert ITERS * U == N_BLOCKS
GROUPS = -(-N_NODES // BLOCK)
N_PAD = GROUPS * BLOCK
BLOCKS_PAD = 512
BASE_MAX = N_PAD - P
HALF = 9
EF_SLOTS = 4
LATE_MIN = GROUPS - (ITERS - 1)
assert GROUPS >= ITERS and BASE_MAX > N_NODES


def build(nc, x, src_cols, dst_cols, dst_blocks, ef_blocks, w_rel_t, w_root_t, b_rel, we1, be1, we2, be2,
          wn1, bn1, wn2, bn2, out):
    h1_rows = nc.dram_tensor("h1_rows", (N_PAD, D), F32, kind="Internal").ap()
    y_rows = nc.dram_tensor("y_rows", (N_PAD, D), F32, kind="Internal").ap()
    lo_dram = nc.dram_tensor("lo_dram", (P, BLOCKS_PAD // P), I32, kind="Internal").ap()
    hi_dram = nc.dram_tensor("hi_dram", (P, BLOCKS_PAD // P), I32, kind="Internal").ap()

    def node_group(rows, g):
        return rows.rearrange("(g t p) f -> g p t f", t=TB, p=P)[bass.ds(g, 1)].rearrange("g p t f -> p (g t) f")

    with ExitStack() as ctx:
        def sb(name, shape, dt=F32):
            return ctx.enter_context(nc.sbuf_tensor(name, shape, dt))

        def bank(name):
            return ctx.enter_context(nc.psum_tensor(name, [P, TB * P], F32))

        def sem(name):
            return ctx.enter_context(nc.semaphore(name))

        agg = [sb("agg0", [P, N_PAD]), sb("agg1", [P, N_PAD])]
        rows = sb("rows", [P, U, TB, D])
        onehot = sb("onehot", [P, 2, TB, P])
        idx = sb("idx", [P, U * TB], I32)
        dst_sb = sb("dst_sb", [P, N_BLOCKS, TB], I32)
        dst_rel = sb("dst_rel", [P, N_BLOCKS, TB])
        blk_sb = sb("blk_sb", [P, BLOCKS_PAD // P, BLOCK], I32)
        lo_sb = sb("lo_sb", [P, BLOCKS_PAD // P], I32)
        hi_sb = sb("hi_sb", [P, BLOCKS_PAD // P], I32)
        base_all = sb("base_all", [P, BLOCKS_PAD], I32)
        hi_row = sb("hi_row", [1, BLOCKS_PAD], I32)
        base_row = sb("base_row", [1, BLOCKS_PAD], I32)
        diff_row = sb("diff_row", [1, BLOCKS_PAD], I32)
        due_row = sb("due_row", [1, N_BLOCKS], I32)
        span = sb("span", [1, 2], I32)
        plan = sb("plan", [1, 2], I32)
        iota_i = sb("iota_i", [P, P], I32)
        part_i = sb("part_i", [P, 1], I32)
        iota_f = sb("iota_f", [P, P])
        part_f = sb("part_f", [P, 1])
        ident = sb("ident", [P, P])
        eps = sb("eps", [P, 1])
        w_rel_sb, w_root_sb = sb("w_rel_sb", [D, D]), sb("w_root_sb", [D, D])
        we1_sb, we2_sb = sb("we1_sb", [D_EDGE, D]), sb("we2_sb", [D, D])
        wn1_sb, wn2_sb = sb("wn1_sb", [D, D]), sb("wn2_sb", [D, D])
        be1_col, bn1_col = sb("be1_col", [D, 1]), sb("bn1_col", [D, 1])
        b_rel_all, be2_all, bn2_all = sb("b_rel_all", [P, D]), sb("be2_all", [P, D]), sb("bn2_all", [P, D])
        e_stats, e_mv = sb("e_stats", [P, U, TB, 6]), sb("e_mv", [P, U, TB, 2])
        e_std, e_rstd, e_shift = sb("e_std", [P, U, TB]), sb("e_rstd", [P, U, TB]), sb("e_shift", [P, U, TB])
        n_stats, n_mv = sb("n_stats", [P, TB, 6]), sb("n_mv", [P, TB, 2])
        n_std, n_rstd, n_shift = sb("n_std", [P, TB]), sb("n_rstd", [P, TB]), sb("n_shift", [P, TB])
        xs, hs, ys = sb("xs", [P, TB, D]), sb("hs", [P, TB, D]), sb("ys", [P, TB, D])
        h1s = sb("h1s", [P, TB, D])
        hT, aggT = sb("hT", [P, TB * P]), sb("aggT", [P, TB * P])
        ef = sb("ef", [D_EDGE, EF_SLOTS, BLOCK])
        hidden = sb("hidden", [P, 2, BLOCK])

        iota_ps, node_t, node_o = bank("iota_ps"), bank("node_t"), bank("node_o")
        seg = [bank("seg_a"), bank("seg_b")]
        hid_ps, ew_ps = bank("hid_ps"), bank("ew_ps")

        s_idx_first, s_idx_a, s_idx_b = sem("s_idx_first"), sem("s_idx_a"), sem("s_idx_b")
        s_dst, s_blk, s_lo_out, s_hi_out = sem("s_dst"), sem("s_blk"), sem("s_lo_out"), sem("s_hi_out")
        s_lohi, s_lohi_back = sem("s_lohi"), sem("s_lohi_back")
        s_wts = sem("s_wts")
        s_iota, s_const, s_setup, s_plan = sem("s_iota"), sem("s_const"), sem("s_setup"), sem("s_plan")
        s_ident, s_pass = sem("s_ident"), sem("s_pass")
        s_rows = [[sem(f"s_rows{l}_{u}") for u in range(U)] for l in range(2)]
        s_seg = [sem("s_seg_done0"), sem("s_seg_done1")]
        s_acc = [sem("s_acc_done0"), sem("s_acc_done1")]
        s_onehot = [sem("s_onehot0"), sem("s_onehot1")]
        s_bn, s_recip, s_add = sem("s_bn"), sem("s_recip"), sem("s_add")
        s_stats, s_std, s_shift, s_h = sem("s_stats"), sem("s_std"), sem("s_shift"), sem("s_h")
        s_ef = [sem(f"s_ef{i}") for i in range(EF_SLOTS)]
        s_hid, s_silu, s_ew, s_msg = sem("s_hid_done"), sem("s_silu"), sem("s_ew_done"), sem("s_msg")
        s_nx, s_nchain, s_nstats, s_nstd = sem("s_nx"), sem("s_nchain"), sem("s_nstats"), sem("s_nstd")
        s_nshift, s_nh, s_nhT, s_nT = sem("s_nshift"), sem("s_nh"), sem("s_nhT"), sem("s_nT")
        s_no, s_nh1, s_ny, s_h1_out, s_y_out = sem("s_no"), sem("s_nh1"), sem("s_ny"), sem("s_h1_out"), sem("s_y_out")
        s_my, s_mhid, s_msilu, s_mo, s_mchain = sem("s_my"), sem("s_mhid"), sem("s_msilu"), sem("s_mo"), sem("s_mchain")
        s_mout, s_out = sem("s_mout"), sem("s_out")

        block = ctx.enter_context(nc.Block())
        N_WTS = 11

        def done(i, u):
            return i * U + (U + u + 1)

        def slot_free(i, u, slots):
            if u >= slots:
                return done(i, u - slots)
            return done(i, max(v for v in range(U) if v % slots == u % slots) - U)

        def hold(eng, s, value):
            eng.wait_ge(s, value)
            eng.nop(nofuse=True)

        def load_plan(eng):
            eng.wait_ge(s_plan, 1)
            passes = eng.value_load(plan[0:1, 0:1], min_val=1, max_val=-(-N_PAD // P) + 1)
            n_late = eng.value_load(plan[0:1, 1:2], min_val=LATE_MIN, max_val=GROUPS)
            return passes, n_late

        def loop_group(it):
            return (it + (GROUPS - 1)) % GROUPS

        def run_all(steps):
            for u in sorted(steps):
                steps[u]()

        def updates(passes, n_late):
            return passes * ITERS + n_late

        @block.sync
        def _(sp):
            def load_idx(it, first, last, s):
                sp.dma_start(idx[:, first * TB:last * TB],
                             src_cols[:, bass.ds(it * (U * TB) + first * TB, (last - first) * TB)]).then_inc(s, 16)

            load_idx(0, 0, HALF, s_idx_a)
            load_idx(0, HALF, U, s_idx_b)
            sp.dma_start(blk_sb[:, :, :], dst_blocks.rearrange("p (c e) -> p c e", e=BLOCK)).then_inc(s_blk, 16)
            sp.dma_start(dst_sb[:, :, :], dst_cols.rearrange("p (k t) -> p k t", t=TB)).then_inc(s_dst, 16)
            sp.wait_ge(s_lohi, 2)
            sp.dma_start(lo_dram, lo_sb[:, :]).then_inc(s_lo_out, 16)
            sp.dma_start(hi_dram, hi_sb[:, :]).then_inc(s_hi_out, 16)
            lo_row = lo_dram.rearrange("p c -> (p c)").rearrange("(a k) -> a k", a=1)
            sp.wait_ge(s_lo_out, 16)
            sp.dma_start(base_row[:, :], lo_row).then_inc(s_lohi_back, 16)
            sp.dma_start(base_all[:, :], lo_row.to_broadcast([P, BLOCKS_PAD])).then_inc(s_lohi_back, 16)
            sp.wait_ge(s_hi_out, 16)
            sp.dma_start(hi_row[:, :], hi_dram.rearrange("p c -> (p c)").rearrange("(a k) -> a k", a=1)
                         ).then_inc(s_lohi_back, 16)
            for dst, w in ((w_rel_sb, w_rel_t), (w_root_sb, w_root_t), (we1_sb, we1), (we2_sb, we2),
                           (wn1_sb, wn1), (wn2_sb, wn2), (be1_col, be1), (bn1_col, bn1)):
                sp.dma_start(dst[:, :], w).then_inc(s_wts, 16)
            for dst, b in ((b_rel_all, b_rel), (be2_all, be2), (bn2_all, bn2)):
                sp.dma_start(dst[:, :], b.to_broadcast([P, D])).then_inc(s_wts, 16)
            passes, n_late = load_plan(sp)

            def node_x(g, n):
                hold(sp, s_ny, n + 1)
                sp.dma_start(xs[:, :, :], node_group(x, g)).then_inc(s_nx, 16)

            with sp.Fori(0, passes) as p:
                with sp.Fori(0, ITERS) as it:
                    i = p * ITERS + it
                    node_x(loop_group(it), i)
                    for u in range(HALF):
                        hold(sp, s_rows[0][u], i * (16 * TB) + 16 * TB)
                    load_idx(it + 1, 0, HALF, s_idx_a)
                    for u in range(HALF, U):
                        hold(sp, s_rows[0][u], i * (16 * TB) + 16 * TB)
                    load_idx(it + 1, HALF, U, s_idx_b)
            with sp.Fori(0, n_late) as j:
                node_x((GROUPS - 1) - j, passes * ITERS + j)

            hold(sp, s_y_out, updates(passes, n_late) * 16)

            def node_y(g, n):
                hold(sp, s_mout, n + 1)
                sp.dma_start(ys[:, :, :], node_group(y_rows, g)).then_inc(s_my, 16)

            with sp.Fori(0, passes) as p:
                with sp.Fori(0, ITERS) as it:
                    i = p * ITERS + it
                    for u in range(U):
                        hold(sp, s_hid, slot_free(i, u, EF_SLOTS))
                        sp.dma_start(ef[:, u % EF_SLOTS, :],
                                     ef_blocks[bass.ds(it * U + u, 1)].rearrange("k c e -> c (k e)")
                                     ).then_inc(s_ef[u % EF_SLOTS], 16)
                        if u == 3:
                            node_y(loop_group(it), i)
                        if u == HALF + 2:
                            for v in range(HALF):
                                hold(sp, s_rows[1][v], i * (16 * TB) + 16 * TB)
                            load_idx(it + 1, 0, HALF, s_idx_a)
                    for v in range(HALF, U):
                        hold(sp, s_rows[1][v], i * (16 * TB) + 16 * TB)
                    load_idx(it + 1, HALF, U, s_idx_b)
            with sp.Fori(0, n_late) as j:
                node_y((GROUPS - 1) - j, passes * ITERS + j)

        @block.gpsimd
        def _(pool):
            nc.gpsimd.iota(iota_i[:, :], pattern=[[1, P]], base=0, channel_multiplier=0)
            nc.gpsimd.iota(part_i[:, :], pattern=[[0, 1]], base=0, channel_multiplier=1)
            nc.gpsimd.iota(due_row[:, :], pattern=[[BLOCK, ITERS], [0, U]], base=0,
                           channel_multiplier=0).then_inc(s_iota, 1)
            passes, n_late = load_plan(pool)

            def gather(layer, table, i, loads_before):
                for u in range(U):
                    if u == 0:
                        hold(pool, s_idx_a, (loads_before + i) * 16 + 16)
                    if u == HALF:
                        hold(pool, s_idx_b, (loads_before + i) * 16 + 16)
                    hold(pool, s_seg[layer], slot_free(i, u, U))
                    for t in range(TB):
                        j = u * TB + t
                        pool.indirect_dma_start(
                            out=rows[:, u, t, :], out_offset=None, in_=table,
                            in_offset=bass.IndirectOffsetOnAxis(ap=idx[:, j:j + 1], axis=0),
                        ).then_inc(s_rows[layer][u], 16)

            with pool.Fori(0, passes) as p:
                with pool.Fori(0, ITERS) as it:
                    gather(0, x, p * ITERS + it, 0)
            hold(pool, s_h1_out, updates(passes, n_late) * 16)
            with pool.Fori(0, passes) as p:
                with pool.Fori(0, ITERS) as it:
                    gather(1, h1_rows, p * ITERS + it, passes * ITERS)

        @block.tensor
        def _(pe):
            pe.sem_inc(s_seg[0], U)
            pe.sem_inc(s_seg[1], U)
            pe.sem_inc(s_hid, U)
            pe.sem_inc(s_ew, U)
            passes, n_late = load_plan(pe)
            pe.wait_ge(s_wts, 16 * N_WTS)
            pe.wait_ge(s_ident, 1)

            def segment_sum(layer, i, u):
                pe.wait_ge(s_acc[layer], slot_free(i, u, 2))
                for t in range(TB):
                    mm = pe.matmul(seg[u % 2][:, 0:P], rows[:, u, t, :], onehot[:, u % 2, t, :],
                                   start=(t == 0), stop=(t == TB - 1))
                mm.then_inc(s_seg[layer], 1)

            def node_update0(n):
                def transpose():
                    pe.wait_ge(s_nh, n + 1)
                    for t in range(TB):
                        tr = pe.transpose(node_t[:, t * P:(t + 1) * P], hs[:, t, :], ident[:, :])
                    tr.then_inc(s_nhT, 1)

                def product():
                    pe.wait_ge(s_nT, n + 1)
                    for t in range(TB):
                        o = node_o[:, t * D:(t + 1) * D]
                        pe.matmul(o, hT[:, t * P:(t + 1) * P], w_root_sb[:, :], start=True, stop=False)
                        mm = pe.matmul(o, aggT[:, t * P:(t + 1) * P], w_rel_sb[:, :], start=False, stop=True)
                    mm.then_inc(s_no, 1)
                return {6: transpose, 8: product}

            with pe.Fori(0, passes) as p:
                with pe.Fori(0, ITERS) as it:
                    i = p * ITERS + it
                    steps = node_update0(i)
                    for u in range(U):
                        pe.wait_ge(s_onehot[0], i * U + u + 1)
                        pe.wait_ge(s_h, i * U + u + 1)
                        segment_sum(0, i, u)
                        if u in steps:
                            steps[u]()
            with pe.Fori(0, n_late) as j:
                run_all(node_update0(passes * ITERS + j))

            def edge_hidden(i, u):
                s, uses = u % EF_SLOTS, len(range(u % EF_SLOTS, U, EF_SLOTS))
                pe.wait_ge(s_ef[s], i * (16 * uses) + 16 * (u // EF_SLOTS + 1))
                pe.matmul(hid_ps[:, :], we1_sb[:, :], ef[:, s, :], start=True, stop=True).then_inc(s_hid, 1)

            def edge_weights(i, u):
                pe.wait_ge(s_silu, i * U + u + 1)
                for t in range(TB):
                    mm = pe.matmul(ew_ps[:, t * D:(t + 1) * D], hidden[:, u % 2, t * P:(t + 1) * P], we2_sb[:, :],
                                   start=True, stop=True)
                mm.then_inc(s_ew, 1)

            def node_update1(g, n, acc_done):
                def hidden_layer():
                    hold(pe, s_acc[1], acc_done)
                    pe.matmul(node_t[:, :], wn1_sb[:, :], agg[1][:, bass.ds(g * BLOCK, BLOCK)],
                              start=True, stop=True).then_inc(s_mhid, 1)

                def product():
                    pe.wait_ge(s_msilu, n + 1)
                    for t in range(TB):
                        mm = pe.matmul(node_o[:, t * D:(t + 1) * D], hT[:, t * P:(t + 1) * P], wn2_sb[:, :],
                                       start=True, stop=True)
                    mm.then_inc(s_mo, 1)
                return {2: hidden_layer, 5: product}

            with pe.Fori(0, passes) as p:
                with pe.Fori(0, ITERS) as it:
                    i = p * ITERS + it
                    steps = node_update1(loop_group(it), i, done(i, -1))
                    edge_hidden(i, 0)
                    for u in range(U):
                        edge_weights(i, u)
                        if u + 1 < U:
                            edge_hidden(i, u + 1)
                        pe.wait_ge(s_msg, i * U + u + 1)
                        segment_sum(1, i, u)
                        if u in steps:
                            steps[u]()
            with pe.Fori(0, n_late) as j:
                run_all(node_update1((GROUPS - 1) - j, passes * ITERS + j, done(passes * ITERS, -1)))

        @block.scalar
        def _(act):
            passes, n_late = load_plan(act)
            act.wait_ge(s_const, 1)
            act.wait_ge(s_wts, 16 * N_WTS)

            def edge_std(i, u):
                act.wait_ge(s_stats, i * U + u + 1)
                nc.scalar.activation(e_std[:, u, :], e_mv[:, u, :, 1], ACT.Sqrt, bias=eps[:, :]).then_inc(s_std, 1)

            def edge_relu(i, u):
                act.wait_ge(s_shift, i * U + u + 1)
                for t in range(TB):
                    op = nc.scalar.activation(rows[:, u, t, :], rows[:, u, t, :], ACT.Relu,
                                              bias=e_shift[:, u, t:t + 1], scale=e_rstd[:, u, t:t + 1])
                op.then_inc(s_h, 1)

            def node_std(c):
                act.wait_ge(s_nstats, c)
                nc.scalar.activation(n_std[:, :], n_mv[:, :, 1], ACT.Sqrt, bias=eps[:, :]).then_inc(s_nstd, 1)

            def node_relu(dst, c, s):
                act.wait_ge(s_nshift, c)
                for t in range(TB):
                    op = nc.scalar.activation(dst[:, t, :], xs[:, t, :], ACT.Relu,
                                              bias=n_shift[:, t:t + 1], scale=n_rstd[:, t:t + 1])
                op.then_inc(s, 1)

            def node_update0(g, n, acc_done):
                def turned():
                    act.wait_ge(s_nhT, n + 1)
                    nc.scalar.activation(hT[:, :], node_t[:, :], ACT.Copy)
                    act.wait_ge(s_acc[0], acc_done)
                    nc.scalar.activation(aggT[:, :], agg[0][:, bass.ds(g * BLOCK, BLOCK)],
                                         ACT.Copy).then_inc(s_nT, 1)

                def h1():
                    node_relu(h1s, n * 2 + 2, s_nh1)
                    act.wait_ge(s_nh1, n + 1)
                    act.dma_start(node_group(h1_rows, g), h1s[:, :, :]).then_inc(s_h1_out, 16)

                def y():
                    act.wait_ge(s_ny, n + 2)
                    act.dma_start(node_group(y_rows, g), ys[:, :, :]).then_inc(s_y_out, 16)

                def stored():
                    act.wait_ge(s_h1_out, n * 16 + 16)
                    act.wait_ge(s_y_out, n * 16 + 16)
                return {3: lambda: node_std(n * 2 + 1), 5: lambda: node_relu(hs, n * 2 + 1, s_nh), 7: turned,
                        10: lambda: node_std(n * 2 + 2), 12: h1, 14: y, 16: stored}

            with act.Fori(0, passes) as p:
                with act.Fori(0, ITERS) as it:
                    i = p * ITERS + it
                    steps = node_update0(loop_group(it), i, done(i, -1))
                    edge_std(i, 0)
                    for u in range(U):
                        edge_relu(i, u)
                        if u + 1 < U:
                            edge_std(i, u + 1)
                        if u in steps:
                            steps[u]()
            with act.Fori(0, n_late) as j:
                run_all(node_update0((GROUPS - 1) - j, passes * ITERS + j, done(passes * ITERS, -1)))

            def node_update1(g, n):
                def hidden_layer():
                    act.wait_ge(s_mhid, n + 1)
                    nc.scalar.activation(hT[:, :], node_t[:, :], ACT.Silu, bias=bn1_col[:, :]).then_inc(s_msilu, 1)

                def result():
                    act.wait_ge(s_mout, n + 2)
                    act.dma_start(node_group(out, g), xs[:, :, :]).then_inc(s_out, 16)

                def stored():
                    act.wait_ge(s_out, n * 16 + 16)
                return {3: hidden_layer, 9: result, 14: stored}

            with act.Fori(0, passes) as p:
                with act.Fori(0, ITERS) as it:
                    i = p * ITERS + it
                    steps = node_update1(loop_group(it), i)
                    for u in range(U):
                        act.wait_ge(s_hid, done(i, u))
                        act.wait_ge(s_ew, slot_free(i, u, 2))
                        nc.scalar.activation(hidden[:, u % 2, :], hid_ps[:, :], ACT.Silu,
                                             bias=be1_col[:, :]).then_inc(s_silu, 1)
                        if u in steps:
                            steps[u]()
            with act.Fori(0, n_late) as j:
                run_all(node_update1((GROUPS - 1) - j, passes * ITERS + j))

        @block.vector
        def _(dve):
            v = nc.vector
            dve.sem_inc(s_acc[0], U)
            dve.sem_inc(s_acc[1], U)
            dve.sem_inc(s_ny, 1)
            dve.sem_inc(s_mout, 1)
            v.memset(eps[:, :], EPS).then_inc(s_const, 1)
            dve.wait_ge(s_iota, 1)
            v.tensor_copy(iota_ps[:, 0:P], iota_i[:, :])
            v.tensor_copy(iota_f[:, :], iota_i[:, :])
            v.tensor_copy(part_f[:, :], part_i[:, :]).then_inc(s_setup, 1)
            dve.wait_ge(s_setup, 1)
            v.tensor_scalar(ident[:, :], iota_f[:, :], part_f[:, 0:1], None, ALU.is_equal).then_inc(s_ident, 1)
            dve.wait_ge(s_blk, 16)
            v.tensor_reduce(lo_sb[:, :], blk_sb[:, :, :], AX.X, ALU.min).then_inc(s_lohi, 1)
            v.tensor_reduce(hi_sb[:, :], blk_sb[:, :, :], AX.X, ALU.max).then_inc(s_lohi, 1)
            v.memset(agg[0][:, :], 0.0)
            dve.wait_ge(s_lohi_back, 48)
            v.tensor_tensor(diff_row[:, :], hi_row[:, :], base_row[:, :], ALU.subtract).then_inc(s_setup, 1)
            dve.wait_ge(s_setup, 2)
            v.tensor_reduce(span[:, 0:1], diff_row[:, :], AX.X, ALU.max).then_inc(s_setup, 1)
            dve.wait_ge(s_setup, 3)
            v.tensor_tensor(diff_row[:, 0:N_BLOCKS], base_row[:, 0:N_BLOCKS], due_row[:, :],
                            ALU.subtract).then_inc(s_setup, 1)
            v.tensor_scalar(plan[:, 0:1], span[:, 0:1], 7, None, ALU.arith_shift_right).then_inc(s_setup, 1)
            dve.wait_ge(s_setup, 5)
            v.tensor_reduce(span[:, 1:2], diff_row[:, 0:N_BLOCKS], AX.X, ALU.min).then_inc(s_setup, 1)
            dve.wait_ge(s_setup, 6)
            v.tensor_scalar(plan[:, 0:1], plan[:, 0:1], 1.0, None, ALU.add).then_inc(s_setup, 1)
            v.tensor_scalar(span[:, 1:2], span[:, 1:2], 0.0, -float(GROUPS - LATE_MIN), ALU.is_ge, ALU.mult).then_inc(s_setup, 1)
            dve.wait_ge(s_setup, 8)
            v.tensor_scalar(plan[:, 1:2], span[:, 1:2], float(GROUPS), None, ALU.add).then_inc(s_plan, 1)
            passes, n_late = load_plan(dve)
            dve.wait_ge(s_dst, 16)

            def window_targets():
                return v.tensor_tensor(dst_rel[:, :, :], dst_sb[:, :, :],
                                       base_all[:, 0:N_BLOCKS].unsqueeze(2).to_broadcast([P, N_BLOCKS, TB]),
                                       ALU.subtract)

            def next_pass(n):
                v.tensor_scalar(dst_rel[:, :, :], dst_rel[:, :, :], float(P), None, ALU.subtract)
                v.tensor_scalar(base_row[:, :], base_row[:, :], float(P), float(BASE_MAX), ALU.add,
                                ALU.min).then_inc(s_pass, 1)
                dve.wait_ge(s_pass, n)

            def one_hot(layer, i, it, u):
                dve.wait_ge(s_seg[layer], slot_free(i, u, 2))
                v.tensor_tensor(onehot[:, u % 2, :, :],
                                iota_ps[:, 0:P].unsqueeze(1).to_broadcast([P, TB, P]),
                                dst_rel[:, bass.ds(it * U + u, 1), :].rearrange("p k t -> p (k t)").unsqueeze(2)
                                .to_broadcast([P, TB, P]),
                                ALU.is_equal).then_inc(s_onehot[layer], 1)

            def add_window(layer, i, it, u):
                base = dve.value_load(base_row[0:1, bass.ds(it * U + u, 1)], min_val=0, max_val=BASE_MAX)
                window = agg[layer][:, bass.ds(base, P)]
                dve.wait_ge(s_seg[layer], done(i, u))
                dve.wait_ge(s_acc[layer], done(i, u - 1))
                v.tensor_tensor(window, seg[u % 2][:, 0:P], window, ALU.add).then_inc(s_acc[layer], 1)

            def edge_stats(i, u):
                dve.wait_ge(s_rows[0][u], i * (16 * TB) + 16 * TB)
                for t in range(TB):
                    op = v.bn_stats(e_stats[:, u, t, :], rows[:, u, t, :])
                op.then_inc(s_bn, 1)
                hold(dve, s_bn, i * U + u + 1)
                for t in range(TB):
                    op = v.bn_aggr(e_mv[:, u, t, :], e_stats[:, u, t, :])
                op.then_inc(s_stats, 1)

            def edge_shift(i, u):
                dve.wait_ge(s_std, i * U + u + 1)
                v.reciprocal(e_rstd[:, u, :], e_std[:, u, :]).then_inc(s_recip, 1)
                dve.wait_ge(s_recip, i * U + u + 1)
                v.scalar_tensor_tensor(e_shift[:, u, :], e_mv[:, u, :, 0], -1.0, e_rstd[:, u, :],
                                       ALU.mult, ALU.mult).then_inc(s_shift, 1)

            def node_stats(c, chain):
                for t in range(TB):
                    op = v.bn_stats(n_stats[:, t, :], xs[:, t, :])
                op.then_inc(s_nchain, 1)
                hold(dve, s_nchain, chain + 1)
                for t in range(TB):
                    op = v.bn_aggr(n_mv[:, t, :], n_stats[:, t, :])
                op.then_inc(s_nstats, 1)

            def node_shift(c, chain):
                dve.wait_ge(s_nstd, c)
                v.reciprocal(n_rstd[:, :], n_std[:, :]).then_inc(s_nchain, 1)
                dve.wait_ge(s_nchain, chain + 1)
                v.scalar_tensor_tensor(n_shift[:, :], n_mv[:, :, 0], -1.0, n_rstd[:, :],
                                       ALU.mult, ALU.mult).then_inc(s_nshift, 1)

            def node_update0(n):
                def stats_x():
                    dve.wait_ge(s_nx, n * 16 + 16)
                    node_stats(n * 2 + 1, n * 6)

                def x1():
                    dve.wait_ge(s_no, n + 1)
                    o = node_o[:, :].rearrange("p (t f) -> p t f", t=TB)
                    v.tensor_tensor(o, o, b_rel_all[:, :].unsqueeze(1).to_broadcast([P, TB, D]),
                                    ALU.add).then_inc(s_nchain, 1)
                    dve.wait_ge(s_nchain, n * 6 + 3)
                    v.tensor_tensor(xs[:, :, :], o, xs[:, :, :], ALU.add).then_inc(s_nchain, 1)
                    dve.wait_ge(s_nchain, n * 6 + 4)
                    node_stats(n * 2 + 2, n * 6 + 4)

                def y():
                    dve.wait_ge(s_nh1, n + 1)
                    v.tensor_tensor(ys[:, :, :], xs[:, :, :], h1s[:, :, :], ALU.add).then_inc(s_ny, 1)
                return {2: stats_x, 4: lambda: node_shift(n * 2 + 1, n * 6 + 1), 9: x1,
                        11: lambda: node_shift(n * 2 + 2, n * 6 + 5), 13: y}

            window_targets().then_inc(s_setup, 1)
            dve.wait_ge(s_setup, 9)
            with dve.Fori(0, passes) as p:
                with dve.Fori(0, ITERS) as it:
                    i = p * ITERS + it
                    steps = node_update0(i)
                    edge_stats(i, 0)
                    edge_stats(i, 1)
                    edge_shift(i, 0)
                    for u in range(U):
                        one_hot(0, i, it, u)
                        if u + 2 < U:
                            edge_stats(i, u + 2)
                        if u + 1 < U:
                            edge_shift(i, u + 1)
                        add_window(0, i, it, u)
                        if u in steps:
                            steps[u]()
                next_pass(p + 1)
            with dve.Fori(0, n_late) as j:
                run_all(node_update0(passes * ITERS + j))

            v.memset(agg[1][:, :], 0.0)
            window_targets()
            v.tensor_copy(base_row[:, :], base_all[0:1, :]).then_inc(s_setup, 1)
            dve.wait_ge(s_setup, 10)

            def message(i, u):
                dve.wait_ge(s_ew, done(i, u))
                ew = ew_ps[:, :].rearrange("p (t f) -> p t f", t=TB)
                v.tensor_tensor(ew, ew, be2_all[:, :].unsqueeze(1).to_broadcast([P, TB, D]),
                                ALU.add).then_inc(s_add, 1)
                dve.wait_ge(s_add, i * U + u + 1)
                dve.wait_ge(s_rows[1][u], i * (16 * TB) + 16 * TB)
                v.tensor_tensor(rows[:, u, :, :], ew, rows[:, u, :, :], ALU.mult).then_inc(s_msg, 1)

            def node_update1(n):
                def result():
                    dve.wait_ge(s_mo, n + 1)
                    o = node_o[:, :].rearrange("p (t f) -> p t f", t=TB)
                    v.tensor_tensor(o, o, bn2_all[:, :].unsqueeze(1).to_broadcast([P, TB, D]),
                                    ALU.add).then_inc(s_mchain, 1)
                    dve.wait_ge(s_mchain, n + 1)
                    dve.wait_ge(s_my, n * 16 + 16)
                    v.tensor_tensor(xs[:, :, :], o, ys[:, :, :], ALU.add).then_inc(s_mout, 1)
                return {8: result}

            with dve.Fori(0, passes) as p:
                with dve.Fori(0, ITERS) as it:
                    i = p * ITERS + it
                    steps = node_update1(i)
                    for u in range(U):
                        one_hot(1, i, it, u)
                        message(i, u)
                        add_window(1, i, it, u)
                        if u in steps:
                            steps[u]()
                next_pass(passes + p + 1)
            with dve.Fori(0, n_late) as j:
                run_all(node_update1(passes * ITERS + j))


def kernel(x, src, dst, edge_attr_50, L0_gnn_W_rel, L0_gnn_W_root, L0_gnn_b_rel, L1_gnn_We1, L1_gnn_be1,
           L1_gnn_We2, L1_gnn_be2, L1_gnn_Wn1, L1_gnn_bn1, L1_gnn_Wn2, L1_gnn_bn2):
    import numpy as np
    import concourse.bacc as bacc
    from concourse.bass_utils import run_bass_kernel_spmd as run

    edges_pad = N_BLOCKS * BLOCK
    x_pad = np.zeros((N_PAD, D), np.float32)
    x_pad[:N_NODES] = x
    src_pad = np.zeros(edges_pad, np.int32)
    src_pad[:N_EDGES] = src
    dst_pad = np.full(BLOCKS_PAD * BLOCK, N_NODES, np.int32)
    dst_pad[:N_EDGES] = dst
    ef_pad = np.zeros((edges_pad, D_EDGE), np.float32)
    ef_pad[:N_EDGES] = edge_attr_50
    src_cols = src_pad.reshape(-1, P).T
    arrays = {
        "x": x_pad,
        "src_cols": np.concatenate([src_cols, src_cols[:, :U * TB]], axis=1),
        "dst_cols": dst_pad[:edges_pad].reshape(-1, P).T,
        "dst_blocks": dst_pad.reshape(P, -1),
        "ef_blocks": ef_pad.reshape(N_BLOCKS, BLOCK, D_EDGE).transpose(0, 2, 1),
        "w_rel_t": np.asarray(L0_gnn_W_rel).T, "w_root_t": np.asarray(L0_gnn_W_root).T,
        "b_rel": np.asarray(L0_gnn_b_rel)[None, :],
        "we1": L1_gnn_We1, "be1": np.asarray(L1_gnn_be1)[:, None],
        "we2": L1_gnn_We2, "be2": np.asarray(L1_gnn_be2)[None, :],
        "wn1": L1_gnn_Wn1, "bn1": np.asarray(L1_gnn_bn1)[:, None],
        "wn2": L1_gnn_Wn2, "bn2": np.asarray(L1_gnn_bn2)[None, :],
    }
    arrays = {name: np.ascontiguousarray(a) for name, a in arrays.items()}
    nc = bacc.Bacc("TRN2", target_bir_lowering=False, num_devices=1)
    args = [nc.dram_tensor(name, a.shape, mybir.dt.from_np(a.dtype), kind="ExternalInput").ap()
            for name, a in arrays.items()]
    out = nc.dram_tensor("out", (N_PAD, D), F32, kind="ExternalOutput").ap()
    build(nc, *args, out)
    got = run(nc, [arrays], core_ids=[0])
    return got.results[0]["out"][:N_NODES]
```

```python
from contextlib import ExitStack

import concourse.bass as bass
from concourse import mybir

F32 = mybir.dt.float32
I32 = mybir.dt.int32
ALU = mybir.AluOpType
ACT = mybir.ActivationFunctionType
AX = mybir.AxisListType

P = 128
N_NODES = 12500
N_EDGES = 200000
D = 128
D_EDGE = 50
EPS = 1e-5
TB = 4
BLOCK = TB * P
N_BLOCKS = -(-N_EDGES // BLOCK)
U = 17
ITERS = N_BLOCKS // U
assert ITERS * U == N_BLOCKS
GROUPS = -(-N_NODES // BLOCK)
N_PAD = GROUPS * BLOCK
BLOCKS_PAD = 512
BASE_MAX = N_PAD - P
HALF = 9
EF_SLOTS = 4
LATE = GROUPS - (ITERS - 1)
LATE_STEPS = -(-GROUPS // LATE)
assert LATE > 0 and BASE_MAX > N_NODES and LATE * LATE_STEPS - GROUPS < LATE


def build(nc, x, src_cols, dst_cols, dst_blocks, ef_blocks, w_rel_t, w_root_t, b_rel, we1, be1, we2, be2,
          wn1, bn1, wn2, bn2, out):
    h1_rows = nc.dram_tensor("h1_rows", (N_PAD, D), F32, kind="Internal").ap()
    y_rows = nc.dram_tensor("y_rows", (N_PAD, D), F32, kind="Internal").ap()
    lo_dram = nc.dram_tensor("lo_dram", (P, BLOCKS_PAD // P), I32, kind="Internal").ap()
    hi_dram = nc.dram_tensor("hi_dram", (P, BLOCKS_PAD // P), I32, kind="Internal").ap()

    def node_group(rows, g):
        return rows.rearrange("(g t p) f -> g p t f", t=TB, p=P)[bass.ds(g, 1)].rearrange("g p t f -> p (g t) f")

    with ExitStack() as ctx:
        def sb(name, shape, dt=F32):
            return ctx.enter_context(nc.sbuf_tensor(name, shape, dt))

        def bank(name):
            return ctx.enter_context(nc.psum_tensor(name, [P, TB * P], F32))

        def sem(name):
            return ctx.enter_context(nc.semaphore(name))

        agg = [sb("agg0", [P, N_PAD]), sb("agg1", [P, N_PAD])]
        rows = sb("rows", [P, U, TB, D])
        onehot = sb("onehot", [P, 2, TB, P])
        idx = sb("idx", [P, U * TB], I32)
        dst_sb = sb("dst_sb", [P, N_BLOCKS, TB], I32)
        dst_rel = sb("dst_rel", [P, N_BLOCKS, TB])
        blk_sb = agg[1][:, 0:BLOCKS_PAD // P * BLOCK].bitcast(I32).rearrange("p (c e) -> p c e", e=BLOCK)
        lo_sb = sb("lo_sb", [P, BLOCKS_PAD // P], I32)
        hi_sb = sb("hi_sb", [P, BLOCKS_PAD // P], I32)
        base_all = sb("base_all", [P, BLOCKS_PAD], I32)
        hi_row = sb("hi_row", [1, BLOCKS_PAD], I32)
        base_row = sb("base_row", [1, BLOCKS_PAD], I32)
        diff_row = sb("diff_row", [1, BLOCKS_PAD], I32)
        due_row = sb("due_row", [1, N_BLOCKS], I32)
        span = sb("span", [1, 2], I32)
        plan = sb("plan", [1, 2], I32)
        iota_i = sb("iota_i", [P, P], I32)
        part_i = sb("part_i", [P, 1], I32)
        iota_f = sb("iota_f", [P, P])
        part_f = sb("part_f", [P, 1])
        ident = sb("ident", [P, P])
        eps = sb("eps", [P, 1])
        w_rel_sb, w_root_sb = sb("w_rel_sb", [D, D]), sb("w_root_sb", [D, D])
        we1_sb, we2_sb = sb("we1_sb", [D_EDGE, D]), sb("we2_sb", [D, D])
        wn1_sb, wn2_sb = sb("wn1_sb", [D, D]), sb("wn2_sb", [D, D])
        be1_col, bn1_col = sb("be1_col", [D, 1]), sb("bn1_col", [D, 1])
        b_rel_all, be2_all, bn2_all = sb("b_rel_all", [P, D]), sb("be2_all", [P, D]), sb("bn2_all", [P, D])
        e_stats, e_mv = sb("e_stats", [P, U, TB, 6]), sb("e_mv", [P, U, TB, 2])
        e_std, e_rstd, e_shift = sb("e_std", [P, U, TB]), sb("e_rstd", [P, U, TB]), sb("e_shift", [P, U, TB])
        n_stats, n_mv = sb("n_stats", [P, LATE, TB, 6]), sb("n_mv", [P, LATE, TB, 2])
        n_std, n_rstd = sb("n_std", [P, LATE, TB]), sb("n_rstd", [P, LATE, TB])
        n_shift = sb("n_shift", [P, LATE, TB])
        xs, ys = sb("xs", [P, LATE, TB, D]), sb("ys", [P, LATE, TB, D])

        def node_sets(name, k):
            return [sb(name, [P, TB, D])[:, :, :]] + [rows[:, (LATE - 1) * k + r, :, :] for r in range(LATE - 1)]

        def flat(sets):
            return [s.rearrange("p t f -> p (t f)") for s in sets]

        hs, h1s = node_sets("hs", 0), node_sets("h1s", 1)
        hT, aggT = flat(node_sets("hT", 2)), flat(node_sets("aggT", 3))
        ef = sb("ef", [D_EDGE, EF_SLOTS, BLOCK])
        hidden = sb("hidden", [P, 2, BLOCK])

        iota_ps = bank("iota_ps")
        seg = [bank("seg_a"), bank("seg_b")]
        hid_ps, ew_ps = bank("hid_ps"), bank("ew_ps")
        node_t, node_o = [bank("node_t"), hid_ps, ew_ps], [bank("node_o"), *seg]
        assert LATE <= 3

        s_idx_a, s_idx_b = sem("s_idx_a"), sem("s_idx_b")
        s_dst, s_blk, s_lo_out, s_hi_out = sem("s_dst"), sem("s_blk"), sem("s_lo_out"), sem("s_hi_out")
        s_lohi, s_lohi_back = sem("s_lohi"), sem("s_lohi_back")
        s_wts = sem("s_wts")
        s_iota, s_const, s_setup, s_plan = sem("s_iota"), sem("s_const"), sem("s_setup"), sem("s_plan")
        s_ident, s_pass = sem("s_ident"), sem("s_pass")
        s_rows = [[sem(f"s_rows{l}_{u}") for u in range(U)] for l in range(2)]
        s_seg = [sem("s_seg_done0"), sem("s_seg_done1")]
        s_acc = [sem("s_acc_done0"), sem("s_acc_done1")]
        s_onehot = [sem("s_onehot0"), sem("s_onehot1")]
        s_bn, s_recip, s_add = sem("s_bn"), sem("s_recip"), sem("s_add")
        s_stats, s_std, s_shift, s_h = sem("s_stats"), sem("s_std"), sem("s_shift"), sem("s_h")
        s_ef = [sem(f"s_ef{i}") for i in range(EF_SLOTS)]
        s_hid, s_silu, s_ew, s_msg = sem("s_hid_done"), sem("s_silu"), sem("s_ew_done"), sem("s_msg")
        s_nx, s_nh, s_nhT, s_nT, s_nbias = sem("s_nx"), sem("s_nh"), sem("s_nhT"), sem("s_nT"), sem("s_nbias")
        s_nx1 = sem("s_nx1")
        s_nbn, s_nstats = [sem("s_nbn0"), sem("s_nbn1")], [sem("s_nstats0"), sem("s_nstats1")]
        s_nstd, s_nrecip = [sem("s_nstd0"), sem("s_nstd1")], [sem("s_nrecip0"), sem("s_nrecip1")]
        s_nshift = [sem("s_nshift0"), sem("s_nshift1")]
        s_no, s_nh1, s_ny, s_h1_out, s_y_out = sem("s_no"), sem("s_nh1"), sem("s_ny"), sem("s_h1_out"), sem("s_y_out")
        s_my, s_mhid, s_msilu, s_mo, s_mbias = sem("s_my"), sem("s_mhid"), sem("s_msilu"), sem("s_mo"), sem("s_mbias")
        s_mout, s_out = sem("s_mout"), sem("s_out")

        block = ctx.enter_context(nc.Block())
        N_WTS = 11

        def done(i, u):
            return i * U + (U + u + 1)

        def slot_free(i, u, slots):
            if u >= slots:
                return done(i, u - slots)
            return done(i, max(v for v in range(U) if v % slots == u % slots) - U)

        def hold(eng, s, value):
            eng.wait_ge(s, value)
            eng.nop(nofuse=True)

        def load_plan(eng):
            eng.wait_ge(s_plan, 1)
            passes = eng.value_load(plan[0:1, 0:1], min_val=1, max_val=-(-N_PAD // P) + 1)
            n_late = eng.value_load(plan[0:1, 1:2], min_val=1, max_val=LATE_STEPS)
            return passes, n_late

        def loop_group(it):
            return (it + (GROUPS - 1)) % GROUPS

        def late_groups(j):
            return [(j * LATE + (GROUPS - LATE + r)) % GROUPS for r in range(LATE)]

        def side_by_side(updates):
            for u in sorted(updates[0]):
                for steps in updates:
                    steps[u]()

        def updates(passes, n_late):
            return passes * ITERS + n_late * LATE

        @block.sync
        def _(sp):
            def load_idx(it, first, last, s):
                sp.dma_start(idx[:, first * TB:last * TB],
                             src_cols[:, bass.ds(it * (U * TB) + first * TB, (last - first) * TB)]).then_inc(s, 16)

            load_idx(0, 0, HALF, s_idx_a)
            load_idx(0, HALF, U, s_idx_b)
            sp.dma_start(blk_sb[:, :, :], dst_blocks.rearrange("p (c e) -> p c e", e=BLOCK)).then_inc(s_blk, 16)
            sp.dma_start(dst_sb[:, :, :], dst_cols.rearrange("p (k t) -> p k t", t=TB)).then_inc(s_dst, 16)
            sp.wait_ge(s_lohi, 2)
            sp.dma_start(lo_dram, lo_sb[:, :]).then_inc(s_lo_out, 16)
            sp.dma_start(hi_dram, hi_sb[:, :]).then_inc(s_hi_out, 16)
            lo_row = lo_dram.rearrange("p c -> (p c)").rearrange("(a k) -> a k", a=1)
            sp.wait_ge(s_lo_out, 16)
            sp.dma_start(base_row[:, :], lo_row).then_inc(s_lohi_back, 16)
            sp.dma_start(base_all[:, :], lo_row.to_broadcast([P, BLOCKS_PAD])).then_inc(s_lohi_back, 16)
            sp.wait_ge(s_hi_out, 16)
            sp.dma_start(hi_row[:, :], hi_dram.rearrange("p c -> (p c)").rearrange("(a k) -> a k", a=1)
                         ).then_inc(s_lohi_back, 16)
            for dst, w in ((w_rel_sb, w_rel_t), (w_root_sb, w_root_t), (we1_sb, we1), (we2_sb, we2),
                           (wn1_sb, wn1), (wn2_sb, wn2), (be1_col, be1), (bn1_col, bn1)):
                sp.dma_start(dst[:, :], w).then_inc(s_wts, 16)
            for dst, b in ((b_rel_all, b_rel), (be2_all, be2), (bn2_all, bn2)):
                sp.dma_start(dst[:, :], b.to_broadcast([P, D])).then_inc(s_wts, 16)
            passes, n_late = load_plan(sp)

            def node_x(groups, n):
                hold(sp, s_ny, n + 1)
                for r, g in enumerate(groups):
                    sp.dma_start(xs[:, r, :, :], node_group(x, g)).then_inc(s_nx, 16)

            with sp.Fori(0, passes) as p:
                with sp.Fori(0, ITERS) as it:
                    i = p * ITERS + it
                    node_x([loop_group(it)], i)
                    for u in range(HALF):
                        hold(sp, s_rows[0][u], i * (16 * TB) + 16 * TB)
                    load_idx(it + 1, 0, HALF, s_idx_a)
                    for u in range(HALF, U):
                        hold(sp, s_rows[0][u], i * (16 * TB) + 16 * TB)
                    load_idx(it + 1, HALF, U, s_idx_b)
            with sp.Fori(0, n_late) as j:
                node_x(late_groups(j), passes * ITERS + j * LATE)

            hold(sp, s_y_out, updates(passes, n_late) * 16)

            def node_y(groups, n):
                hold(sp, s_mout, n + 1)
                for r, g in enumerate(groups):
                    sp.dma_start(ys[:, r, :, :], node_group(y_rows, g)).then_inc(s_my, 16)

            with sp.Fori(0, passes) as p:
                with sp.Fori(0, ITERS) as it:
                    i = p * ITERS + it
                    for u in range(U):
                        hold(sp, s_hid, slot_free(i, u, EF_SLOTS))
                        sp.dma_start(ef[:, u % EF_SLOTS, :],
                                     ef_blocks[bass.ds(it * U + u, 1)].rearrange("k c e -> c (k e)")
                                     ).then_inc(s_ef[u % EF_SLOTS], 16)
                        if u == 3:
                            node_y([loop_group(it)], i)
                        if u == HALF + 2:
                            for v in range(HALF):
                                hold(sp, s_rows[1][v], i * (16 * TB) + 16 * TB)
                            load_idx(it + 1, 0, HALF, s_idx_a)
                    for v in range(HALF, U):
                        hold(sp, s_rows[1][v], i * (16 * TB) + 16 * TB)
                    load_idx(it + 1, HALF, U, s_idx_b)
            with sp.Fori(0, n_late) as j:
                node_y(late_groups(j), passes * ITERS + j * LATE)

        @block.gpsimd
        def _(pool):
            nc.gpsimd.iota(iota_i[:, :], pattern=[[1, P]], base=0, channel_multiplier=0)
            nc.gpsimd.iota(part_i[:, :], pattern=[[0, 1]], base=0, channel_multiplier=1)
            nc.gpsimd.iota(due_row[:, :], pattern=[[BLOCK, ITERS], [0, U]], base=0,
                           channel_multiplier=0).then_inc(s_iota, 1)
            passes_so_far = pool.alloc_register("passes_so_far")
            pool.reg_mov(passes_so_far, 1)

            def gather(layer, table, i, loads_before):
                for u in range(U):
                    if u == 0:
                        hold(pool, s_idx_a, (loads_before + i) * 16 + 16)
                    if u == HALF:
                        hold(pool, s_idx_b, (loads_before + i) * 16 + 16)
                    hold(pool, s_seg[layer], slot_free(i, u, U))
                    for t in range(TB):
                        j = u * TB + t
                        pool.indirect_dma_start(
                            out=rows[:, u, t, :], out_offset=None, in_=table,
                            in_offset=bass.IndirectOffsetOnAxis(ap=idx[:, j:j + 1], axis=0),
                        ).then_inc(s_rows[layer][u], 16)

            with pool.Fori(0, passes_so_far) as p:
                with pool.Fori(0, ITERS) as it:
                    gather(0, x, p * ITERS + it, 0)
                hold(pool, s_plan, 1)
                pool.reg_load(passes_so_far, plan[0:1, 0:1])
            passes, n_late = load_plan(pool)
            hold(pool, s_h1_out, updates(passes, n_late) * 16)
            hold(pool, s_ny, updates(passes, n_late) + 1)
            with pool.Fori(0, passes) as p:
                with pool.Fori(0, ITERS) as it:
                    gather(1, h1_rows, p * ITERS + it, passes * ITERS)

        @block.tensor
        def _(pe):
            pe.sem_inc(s_seg[0], U)
            pe.sem_inc(s_seg[1], U)
            pe.sem_inc(s_hid, U)
            pe.sem_inc(s_ew, U)
            passes, n_late = load_plan(pe)
            pe.wait_ge(s_wts, 16 * N_WTS)
            pe.wait_ge(s_ident, 1)

            def segment_sum(layer, i, u):
                pe.wait_ge(s_acc[layer], slot_free(i, u, 2))
                for t in range(TB):
                    mm = pe.matmul(seg[u % 2][:, 0:P], rows[:, u, t, :], onehot[:, u % 2, t, :],
                                   start=(t == 0), stop=(t == TB - 1))
                mm.then_inc(s_seg[layer], 1)

            def node_update0(n, r):
                def transpose():
                    pe.wait_ge(s_nh, n + 1)
                    for t in range(TB):
                        tr = pe.transpose(node_t[r][:, t * P:(t + 1) * P], hs[r][:, t, :], ident[:, :])
                    tr.then_inc(s_nhT, 1)

                def product():
                    pe.wait_ge(s_nT, n + 1)
                    for t in range(TB):
                        o = node_o[r][:, t * D:(t + 1) * D]
                        pe.matmul(o, hT[r][:, t * P:(t + 1) * P], w_root_sb[:, :], start=True, stop=False)
                        mm = pe.matmul(o, aggT[r][:, t * P:(t + 1) * P], w_rel_sb[:, :], start=False, stop=True)
                    mm.then_inc(s_no, 1)
                return {7: transpose, 9: product}

            with pe.Fori(0, passes) as p:
                with pe.Fori(0, ITERS) as it:
                    i = p * ITERS + it
                    steps = node_update0(i, 0)
                    for u in range(U):
                        if u in steps:
                            steps[u]()
                        pe.wait_ge(s_onehot[0], i * U + u + 1)
                        pe.wait_ge(s_h, i * U + u + 1)
                        segment_sum(0, i, u)
            hold(pe, s_acc[0], done(passes * ITERS, -1))
            with pe.Fori(0, n_late) as j:
                side_by_side([node_update0(passes * ITERS + j * LATE + r, r) for r in range(LATE)])

            def edge_hidden(i, u):
                s, uses = u % EF_SLOTS, len(range(u % EF_SLOTS, U, EF_SLOTS))
                pe.wait_ge(s_ef[s], i * (16 * uses) + 16 * (u // EF_SLOTS + 1))
                pe.matmul(hid_ps[:, :], we1_sb[:, :], ef[:, s, :], start=True, stop=True).then_inc(s_hid, 1)

            def edge_weights(i, u):
                pe.wait_ge(s_silu, i * U + u + 1)
                for t in range(TB):
                    mm = pe.matmul(ew_ps[:, t * D:(t + 1) * D], hidden[:, u % 2, t * P:(t + 1) * P], we2_sb[:, :],
                                   start=True, stop=True)
                mm.then_inc(s_ew, 1)

            HIDDEN_AT = 2

            def node_update1(g, n, r, acc_done):
                def hidden_layer():
                    hold(pe, s_acc[1], acc_done)
                    pe.matmul(node_t[r][:, :], wn1_sb[:, :], agg[1][:, bass.ds(g * BLOCK, BLOCK)],
                              start=True, stop=True).then_inc(s_mhid, 1)

                def product():
                    pe.wait_ge(s_msilu, n + 1)
                    for t in range(TB):
                        mm = pe.matmul(node_o[r][:, t * D:(t + 1) * D], hT[r][:, t * P:(t + 1) * P], wn2_sb[:, :],
                                       start=True, stop=True)
                    mm.then_inc(s_mo, 1)
                return {HIDDEN_AT: hidden_layer, 5: product}

            with pe.Fori(0, passes) as p:
                with pe.Fori(0, ITERS) as it:
                    i = p * ITERS + it
                    steps = node_update1(loop_group(it), i, 0, done(i, HIDDEN_AT - 1))
                    edge_hidden(i, 0)
                    for u in range(U):
                        edge_weights(i, u)
                        if u + 1 < U:
                            edge_hidden(i, u + 1)
                        if u in steps:
                            steps[u]()
                        pe.wait_ge(s_msg, i * U + u + 1)
                        segment_sum(1, i, u)
            with pe.Fori(0, n_late) as j:
                side_by_side([node_update1(g, passes * ITERS + j * LATE + r, r, done(passes * ITERS, -1))
                              for r, g in enumerate(late_groups(j))])

        @block.scalar
        def _(act):
            passes, n_late = load_plan(act)
            act.wait_ge(s_const, 1)
            act.wait_ge(s_wts, 16 * N_WTS)

            def edge_std(i, u):
                act.wait_ge(s_stats, i * U + u + 1)
                nc.scalar.activation(e_std[:, u, :], e_mv[:, u, :, 1], ACT.Sqrt, bias=eps[:, :]).then_inc(s_std, 1)

            def edge_relu(i, u):
                act.wait_ge(s_shift, i * U + u + 1)
                for t in range(TB):
                    op = nc.scalar.activation(rows[:, u, t, :], rows[:, u, t, :], ACT.Relu,
                                              bias=e_shift[:, u, t:t + 1], scale=e_rstd[:, u, t:t + 1])
                op.then_inc(s_h, 1)

            def node_std(n, r, ln):
                act.wait_ge(s_nstats[ln], n + 1)
                nc.scalar.activation(n_std[:, r, :], n_mv[:, r, :, 1], ACT.Sqrt, bias=eps[:, :]).then_inc(s_nstd[ln], 1)

            def node_relu(dst, n, r, ln):
                act.wait_ge(s_nshift[ln], n + 1)
                for t in range(TB):
                    op = nc.scalar.activation(dst[:, t, :], xs[:, r, t, :], ACT.Relu,
                                              bias=n_shift[:, r, t:t + 1], scale=n_rstd[:, r, t:t + 1])
                op.then_inc((s_nh, s_nh1)[ln], 1)

            TURN_AT = 8

            def node_update0(g, n, r, acc_done, issued):
                def turned():
                    act.wait_ge(s_nhT, n + 1)
                    nc.scalar.activation(hT[r], node_t[r][:, :], ACT.Copy)
                    act.wait_ge(s_acc[0], acc_done)
                    nc.scalar.activation(aggT[r], agg[0][:, bass.ds(g * BLOCK, BLOCK)],
                                         ACT.Copy).then_inc(s_nT, 1)

                def h1():
                    node_relu(h1s[r], n, r, 1)
                    act.wait_ge(s_nh1, n + 1)
                    act.dma_start(node_group(h1_rows, g), h1s[r]).then_inc(s_h1_out, 16)

                def y():
                    act.wait_ge(s_ny, n + 2)
                    act.dma_start(node_group(y_rows, g), ys[:, r, :, :]).then_inc(s_y_out, 16)

                def stored():
                    act.wait_ge(s_h1_out, issued * 16)
                    act.wait_ge(s_y_out, issued * 16)
                return {4: lambda: node_std(n, r, 0), 6: lambda: node_relu(hs[r], n, r, 0), TURN_AT: turned,
                        11: lambda: node_std(n, r, 1), 13: h1, 15: y, 16: stored}

            with act.Fori(0, passes) as p:
                with act.Fori(0, ITERS) as it:
                    i = p * ITERS + it
                    steps = node_update0(loop_group(it), i, 0, done(i, TURN_AT - 1), i + 1)
                    edge_std(i, 0)
                    for u in range(U):
                        if u in steps:
                            steps[u]()
                        edge_relu(i, u)
                        if u + 1 < U:
                            edge_std(i, u + 1)
            hold(act, s_seg[0], done(passes * ITERS, -1))
            with act.Fori(0, n_late) as j:
                n = passes * ITERS + j * LATE
                side_by_side([node_update0(g, n + r, r, done(passes * ITERS, -1), n + LATE)
                              for r, g in enumerate(late_groups(j))])

            def node_update1(g, n, r, issued):
                def hidden_layer():
                    act.wait_ge(s_mhid, n + 1)
                    nc.scalar.activation(hT[r], node_t[r][:, :], ACT.Silu, bias=bn1_col[:, :]).then_inc(s_msilu, 1)

                def result():
                    act.wait_ge(s_mout, n + 2)
                    act.dma_start(node_group(out, g), xs[:, r, :, :]).then_inc(s_out, 16)

                def stored():
                    act.wait_ge(s_out, issued * 16)
                return {3: hidden_layer, 9: result, 14: stored}

            with act.Fori(0, passes) as p:
                with act.Fori(0, ITERS) as it:
                    i = p * ITERS + it
                    steps = node_update1(loop_group(it), i, 0, i + 1)
                    for u in range(U):
                        act.wait_ge(s_hid, done(i, u))
                        act.wait_ge(s_ew, slot_free(i, u, 2))
                        nc.scalar.activation(hidden[:, u % 2, :], hid_ps[:, :], ACT.Silu,
                                             bias=be1_col[:, :]).then_inc(s_silu, 1)
                        if u in steps:
                            steps[u]()
            with act.Fori(0, n_late) as j:
                n = passes * ITERS + j * LATE
                side_by_side([node_update1(g, n + r, r, n + LATE) for r, g in enumerate(late_groups(j))])

        @block.vector
        def _(dve):
            v = nc.vector
            dve.sem_inc(s_acc[0], U)
            dve.sem_inc(s_acc[1], U)
            dve.sem_inc(s_ny, 1)
            dve.sem_inc(s_mout, 1)
            v.memset(eps[:, :], EPS).then_inc(s_const, 1)
            dve.wait_ge(s_iota, 1)
            v.tensor_copy(iota_ps[:, 0:P], iota_i[:, :])
            v.tensor_copy(iota_f[:, :], iota_i[:, :])
            v.tensor_copy(part_f[:, :], part_i[:, :]).then_inc(s_setup, 1)
            dve.wait_ge(s_setup, 1)
            v.tensor_scalar(ident[:, :], iota_f[:, :], part_f[:, 0:1], None, ALU.is_equal).then_inc(s_ident, 1)
            dve.wait_ge(s_blk, 16)
            v.tensor_reduce(lo_sb[:, :], blk_sb[:, :, :], AX.X, ALU.min).then_inc(s_lohi, 1)
            v.tensor_reduce(hi_sb[:, :], blk_sb[:, :, :], AX.X, ALU.max).then_inc(s_lohi, 1)
            v.memset(agg[0][:, :], 0.0)
            dve.wait_ge(s_lohi_back, 48)
            v.tensor_tensor(diff_row[:, :], hi_row[:, :], base_row[:, :], ALU.subtract).then_inc(s_setup, 1)
            dve.wait_ge(s_setup, 2)
            v.tensor_reduce(span[:, 0:1], diff_row[:, :], AX.X, ALU.max).then_inc(s_setup, 1)
            dve.wait_ge(s_setup, 3)
            v.tensor_tensor(diff_row[:, 0:N_BLOCKS], base_row[:, 0:N_BLOCKS], due_row[:, :],
                            ALU.subtract).then_inc(s_setup, 1)
            v.tensor_scalar(plan[:, 0:1], span[:, 0:1], 7, None, ALU.arith_shift_right).then_inc(s_setup, 1)
            dve.wait_ge(s_setup, 5)
            v.tensor_reduce(span[:, 1:2], diff_row[:, 0:N_BLOCKS], AX.X, ALU.min).then_inc(s_setup, 1)
            dve.wait_ge(s_setup, 6)
            v.tensor_scalar(plan[:, 0:1], plan[:, 0:1], 1.0, None, ALU.add).then_inc(s_setup, 1)
            v.tensor_scalar(span[:, 1:2], span[:, 1:2], 0.0, 1.0 - LATE_STEPS, ALU.is_ge, ALU.mult).then_inc(s_setup, 1)
            dve.wait_ge(s_setup, 8)
            v.tensor_scalar(plan[:, 1:2], span[:, 1:2], float(LATE_STEPS), None, ALU.add).then_inc(s_plan, 1)
            passes, n_late = load_plan(dve)
            dve.wait_ge(s_dst, 16)

            def window_targets():
                return v.tensor_tensor(dst_rel[:, :, :], dst_sb[:, :, :],
                                       base_all[:, 0:N_BLOCKS].unsqueeze(2).to_broadcast([P, N_BLOCKS, TB]),
                                       ALU.subtract)

            def next_pass(n):
                v.tensor_scalar(dst_rel[:, :, :], dst_rel[:, :, :], float(P), None, ALU.subtract)
                v.tensor_scalar(base_row[:, :], base_row[:, :], float(P), float(BASE_MAX), ALU.add,
                                ALU.min).then_inc(s_pass, 1)
                dve.wait_ge(s_pass, n)

            def one_hot(layer, i, it, u):
                dve.wait_ge(s_seg[layer], slot_free(i, u, 2))
                v.tensor_tensor(onehot[:, u % 2, :, :],
                                iota_ps[:, 0:P].unsqueeze(1).to_broadcast([P, TB, P]),
                                dst_rel[:, bass.ds(it * U + u, 1), :].rearrange("p k t -> p (k t)").unsqueeze(2)
                                .to_broadcast([P, TB, P]),
                                ALU.is_equal).then_inc(s_onehot[layer], 1)

            def add_window(layer, i, it, u):
                base = dve.value_load(base_row[0:1, bass.ds(it * U + u, 1)], min_val=0, max_val=BASE_MAX)
                window = agg[layer][:, bass.ds(base, P)]
                dve.wait_ge(s_seg[layer], done(i, u))
                dve.wait_ge(s_acc[layer], done(i, u - 1))
                v.tensor_tensor(window, seg[u % 2][:, 0:P], window, ALU.add).then_inc(s_acc[layer], 1)

            def edge_stats(i, u):
                dve.wait_ge(s_rows[0][u], i * (16 * TB) + 16 * TB)
                for t in range(TB):
                    op = v.bn_stats(e_stats[:, u, t, :], rows[:, u, t, :])
                op.then_inc(s_bn, 1)
                hold(dve, s_bn, i * U + u + 1)
                for t in range(TB):
                    op = v.bn_aggr(e_mv[:, u, t, :], e_stats[:, u, t, :])
                op.then_inc(s_stats, 1)

            def edge_shift(i, u):
                dve.wait_ge(s_std, i * U + u + 1)
                v.reciprocal(e_rstd[:, u, :], e_std[:, u, :]).then_inc(s_recip, 1)
                dve.wait_ge(s_recip, i * U + u + 1)
                v.scalar_tensor_tensor(e_shift[:, u, :], e_mv[:, u, :, 0], -1.0, e_rstd[:, u, :],
                                       ALU.mult, ALU.mult).then_inc(s_shift, 1)

            def node_stats(n, r, ln):
                for t in range(TB):
                    op = v.bn_stats(n_stats[:, r, t, :], xs[:, r, t, :])
                op.then_inc(s_nbn[ln], 1)
                hold(dve, s_nbn[ln], n + 1)
                for t in range(TB):
                    op = v.bn_aggr(n_mv[:, r, t, :], n_stats[:, r, t, :])
                op.then_inc(s_nstats[ln], 1)

            def node_shift(n, r, ln):
                dve.wait_ge(s_nstd[ln], n + 1)
                v.reciprocal(n_rstd[:, r, :], n_std[:, r, :]).then_inc(s_nrecip[ln], 1)
                dve.wait_ge(s_nrecip[ln], n + 1)
                v.scalar_tensor_tensor(n_shift[:, r, :], n_mv[:, r, :, 0], -1.0, n_rstd[:, r, :],
                                       ALU.mult, ALU.mult).then_inc(s_nshift[ln], 1)

            def node_update0(n, r, loaded):
                def stats_x():
                    dve.wait_ge(s_nx, loaded * 16)
                    node_stats(n, r, 0)

                def x1():
                    dve.wait_ge(s_no, n + 1)
                    o = node_o[r][:, :].rearrange("p (t f) -> p t f", t=TB)
                    v.tensor_tensor(o, o, b_rel_all[:, :].unsqueeze(1).to_broadcast([P, TB, D]),
                                    ALU.add).then_inc(s_nbias, 1)
                    dve.wait_ge(s_nbias, n + 1)
                    v.tensor_tensor(xs[:, r, :, :], o, xs[:, r, :, :], ALU.add).then_inc(s_nx1, 1)
                    dve.wait_ge(s_nx1, n + 1)
                    node_stats(n, r, 1)

                def y():
                    dve.wait_ge(s_nh1, n + 1)
                    v.tensor_tensor(ys[:, r, :, :], xs[:, r, :, :], h1s[r], ALU.add).then_inc(s_ny, 1)
                return {2: stats_x, 4: lambda: node_shift(n, r, 0), 9: x1, 11: lambda: node_shift(n, r, 1), 13: y}

            window_targets().then_inc(s_setup, 1)
            dve.wait_ge(s_setup, 9)
            with dve.Fori(0, passes) as p:
                with dve.Fori(0, ITERS) as it:
                    i = p * ITERS + it
                    steps = node_update0(i, 0, i + 1)
                    edge_stats(i, 0)
                    edge_stats(i, 1)
                    edge_shift(i, 0)
                    for u in range(U):
                        one_hot(0, i, it, u)
                        if u + 2 < U:
                            edge_stats(i, u + 2)
                        if u + 1 < U:
                            edge_shift(i, u + 1)
                        add_window(0, i, it, u)
                        if u in steps:
                            steps[u]()
                next_pass(p + 1)
            with dve.Fori(0, n_late) as j:
                n = passes * ITERS + j * LATE
                side_by_side([node_update0(n + r, r, n + LATE) for r in range(LATE)])

            v.memset(agg[1][:, :], 0.0)
            window_targets()
            v.tensor_copy(base_row[:, :], base_all[0:1, :]).then_inc(s_setup, 1)
            dve.wait_ge(s_setup, 10)

            def message(i, u):
                dve.wait_ge(s_ew, done(i, u))
                ew = ew_ps[:, :].rearrange("p (t f) -> p t f", t=TB)
                v.tensor_tensor(ew, ew, be2_all[:, :].unsqueeze(1).to_broadcast([P, TB, D]),
                                ALU.add).then_inc(s_add, 1)
                dve.wait_ge(s_add, i * U + u + 1)
                dve.wait_ge(s_rows[1][u], i * (16 * TB) + 16 * TB)
                v.tensor_tensor(rows[:, u, :, :], ew, rows[:, u, :, :], ALU.mult).then_inc(s_msg, 1)

            def node_update1(n, r, loaded):
                def result():
                    dve.wait_ge(s_mo, n + 1)
                    o = node_o[r][:, :].rearrange("p (t f) -> p t f", t=TB)
                    v.tensor_tensor(o, o, bn2_all[:, :].unsqueeze(1).to_broadcast([P, TB, D]),
                                    ALU.add).then_inc(s_mbias, 1)
                    dve.wait_ge(s_mbias, n + 1)
                    dve.wait_ge(s_my, loaded * 16)
                    v.tensor_tensor(xs[:, r, :, :], o, ys[:, r, :, :], ALU.add).then_inc(s_mout, 1)
                return {8: result}

            with dve.Fori(0, passes) as p:
                with dve.Fori(0, ITERS) as it:
                    i = p * ITERS + it
                    steps = node_update1(i, 0, i + 1)
                    for u in range(U):
                        one_hot(1, i, it, u)
                        message(i, u)
                        add_window(1, i, it, u)
                        if u in steps:
                            steps[u]()
                next_pass(passes + p + 1)
            with dve.Fori(0, n_late) as j:
                n = passes * ITERS + j * LATE
                side_by_side([node_update1(n + r, r, n + LATE) for r in range(LATE)])


def kernel(x, src, dst, edge_attr_50, L0_gnn_W_rel, L0_gnn_W_root, L0_gnn_b_rel, L1_gnn_We1, L1_gnn_be1,
           L1_gnn_We2, L1_gnn_be2, L1_gnn_Wn1, L1_gnn_bn1, L1_gnn_Wn2, L1_gnn_bn2):
    import numpy as np
    import concourse.bacc as bacc
    from concourse.bass_utils import run_bass_kernel_spmd as run

    edges_pad = N_BLOCKS * BLOCK
    x_pad = np.zeros((N_PAD, D), np.float32)
    x_pad[:N_NODES] = x
    src_pad = np.zeros(edges_pad, np.int32)
    src_pad[:N_EDGES] = src
    dst_pad = np.full(BLOCKS_PAD * BLOCK, N_NODES, np.int32)
    dst_pad[:N_EDGES] = dst
    ef_pad = np.zeros((edges_pad, D_EDGE), np.float32)
    ef_pad[:N_EDGES] = edge_attr_50
    src_cols = src_pad.reshape(-1, P).T
    arrays = {
        "x": x_pad,
        "src_cols": np.concatenate([src_cols, src_cols[:, :U * TB]], axis=1),
        "dst_cols": dst_pad[:edges_pad].reshape(-1, P).T,
        "dst_blocks": dst_pad.reshape(P, -1),
        "ef_blocks": ef_pad.reshape(N_BLOCKS, BLOCK, D_EDGE).transpose(0, 2, 1),
        "w_rel_t": np.asarray(L0_gnn_W_rel).T, "w_root_t": np.asarray(L0_gnn_W_root).T,
        "b_rel": np.asarray(L0_gnn_b_rel)[None, :],
        "we1": L1_gnn_We1, "be1": np.asarray(L1_gnn_be1)[:, None],
        "we2": L1_gnn_We2, "be2": np.asarray(L1_gnn_be2)[None, :],
        "wn1": L1_gnn_Wn1, "bn1": np.asarray(L1_gnn_bn1)[:, None],
        "wn2": L1_gnn_Wn2, "bn2": np.asarray(L1_gnn_bn2)[None, :],
    }
    arrays = {name: np.ascontiguousarray(a) for name, a in arrays.items()}
    nc = bacc.Bacc("TRN2", target_bir_lowering=False, num_devices=1)
    args = [nc.dram_tensor(name, a.shape, mybir.dt.from_np(a.dtype), kind="ExternalInput").ap()
            for name, a in arrays.items()]
    out = nc.dram_tensor("out", (N_PAD, D), F32, kind="ExternalOutput").ap()
    build(nc, *args, out)
    got = run(nc, [arrays], core_ids=[0])
    return got.results[0]["out"][:N_NODES]
```
